# Optimizing a Trainium2 kernel written in Bass

```python
import numpy as np
import jax
import jax.numpy as jnp

def _softmax(x, axis=-1):
    return jax.nn.softmax(x, axis=axis)

def _gelu(x):
    return jax.nn.gelu(x, approximate=True)

def _silu(x):
    return jax.nn.silu(x)

def _sigmoid(x):
    return jax.nn.sigmoid(x)

def _layernorm(x, axis=-1, eps=1e-05):
    m = jnp.mean(x, axis=axis, keepdims=True)
    v = jnp.var(x, axis=axis, keepdims=True)
    return (x - m) / jnp.sqrt(v + eps)

def _scatter_add(tgt, idx, src, axis=0):
    return tgt.at[idx].add(src)

def _segment_sum(src, seg, n):
    return jax.ops.segment_sum(src, seg, n)
kernel_name = 'mk_decoder_preln_d1_seqx_r8_1fa57f'

def setup_inputs(seed: int=0):
    np.random.seed(seed)
    _w = jnp.asarray

    def _rec_inputs():
        import jax
        import jax.numpy as jnp
        _rk = jax.random.key(seed)
        x = 7.22e-05 + 1 * jax.random.normal(jax.random.fold_in(_rk, 1), (8, 128, 512), jnp.float32)
        _lenS = 128 - jax.random.randint(jax.random.fold_in(_rk, 7), (8,), 0, max(1, 128 // 4) + 1, jnp.int32)
        _lenS2 = 128 - jax.random.randint(jax.random.fold_in(_rk, 8), (8,), 0, max(1, 128 // 4) + 1, jnp.int32)
        _ctx_4096P = jax.random.normal(jax.random.fold_in(_rk, 11), (8, 16, 512), jnp.float32)
        _ctx_4096c = jax.random.dirichlet(jax.random.fold_in(_rk, 511), 0.3 * jnp.ones((16,), jnp.float32), (8, 128))
        _ctx_4096t = jnp.einsum('bsk,bkd->bsd', _ctx_4096c, _ctx_4096P)
        _ctx_4096t = _ctx_4096t * jax.lax.rsqrt(jnp.mean(jnp.square(_ctx_4096t)) + 1e-12) * 0.953939
        ctx_4096 = 4.13588e-05 + 0.999923 * (_ctx_4096t + 0.3 * jax.random.normal(jax.random.fold_in(_rk, 611), (8, 128, 512), jnp.float32))
        _validS = jnp.arange(128)[None, :] < _lenS[:, None]
        _validS2 = jnp.arange(128)[None, :] < _lenS2[:, None]
        _causal = jnp.tril(jnp.ones((128, 128), dtype=bool))
        mask_BxSxS2_bk0 = jnp.logical_not(jnp.broadcast_to(_validS2[:, None, :], (8, 128, 128)))
        return (x, ctx_4096, mask_BxSxS2_bk0)
    x, ctx_4096, mask_BxSxS2_bk0 = _rec_inputs()

    def _L0_attn_setup():
        import jax, jax.numpy as jnp
        import numpy as np
        import math
        DIM, NH, NKV, HD = (512, 32, 8, 128)
        BLOCK, NBLK, TOPK = (32, 128, 16)

        def apply_rope(x, cos, sin):
            b, l, h, d = x.shape
            xr = x.reshape(b, l, h, d // 2, 2)
            xe, xo = (xr[..., 0], xr[..., 1])
            c = cos[None, :, None, :]
            s = sin[None, :, None, :]
            oe = xe * c - xo * s
            oo = xe * s + xo * c
            return jnp.stack([oe, oo], axis=-1).reshape(b, l, h, d)
        key = jax.random.key(seed)
        ks = jax.random.split(key, 8)
        x = jax.random.normal(ks[0], (1, 1, DIM), dtype=jnp.float32)
        start_pos = 512
        inv_freq = 1.0 / 500000.0 ** (np.arange(0, HD, 2, dtype=np.float32) / HD)
        ang = np.float32(start_pos) * inv_freq
        freqs_cos = jnp.asarray(np.cos(ang))[None, :]
        freqs_sin = jnp.asarray(np.sin(ang))[None, :]
        sc = 0.02
        wq = jax.random.normal(ks[1], (NH * HD, DIM), dtype=jnp.float32) * sc
        wk = jax.random.normal(ks[2], (NKV * HD, DIM), dtype=jnp.float32) * sc
        wv = jax.random.normal(ks[3], (NKV * HD, DIM), dtype=jnp.float32) * sc
        wo = jax.random.normal(ks[4], (DIM, NH * HD), dtype=jnp.float32) * sc
        k_cache = jax.random.normal(ks[5], (NBLK, BLOCK, NKV, HD), dtype=jnp.float32)
        v_cache = jax.random.normal(ks[6], (NBLK, BLOCK, NKV, HD), dtype=jnp.float32)
        block_idx = jnp.sort(jax.random.randint(ks[7], (TOPK,), 0, NBLK, dtype=jnp.int32))
        return {'x': x, 'freqs_cos': freqs_cos, 'freqs_sin': freqs_sin, 'wq': wq, 'wk': wk, 'wv': wv, 'wo': wo, 'k_cache': k_cache, 'v_cache': v_cache, 'block_idx': block_idx}
    _L0_attn_all = _L0_attn_setup()
    _L0_attn_in = {k: v for k, v in _L0_attn_all.items() if k in ('freqs_cos', 'freqs_sin', 'wq', 'wk', 'wv', 'wo', 'k_cache', 'v_cache', 'block_idx')}
    del _L0_attn_all

    def _L0_xattn_setup():
        import jax, jax.numpy as jnp
        import numpy as np
        B, LQ, LK, D, H, DH = (2, 128, 128, 512, 32, 128)
        EPS = 1e-05

        def _rmsnorm(x, weight):
            var = jnp.mean(jnp.square(x), axis=-1, keepdims=True)
            return x * jax.lax.rsqrt(var + EPS) * weight
        key = jax.random.key(seed)
        ks = jax.random.split(key, 8)
        scale = 0.02
        return {'hidden_states': jax.random.normal(ks[0], (B, LQ, D), jnp.float32), 'key_value_states': jax.random.normal(ks[1], (B, LK, D), jnp.float32), 'attention_mask': jax.random.randint(ks[2], (B, LQ, LK), 0, 2) > 0, 'position_bias': jax.random.normal(ks[3], (H, LQ, LK), jnp.float32), 'ln_weight': jnp.ones((D,), jnp.float32), 'w_q': jax.random.normal(ks[4], (H * DH, D), jnp.float32) * scale, 'w_k': jax.random.normal(ks[5], (H * DH, D), jnp.float32) * scale, 'w_v': jax.random.normal(ks[6], (H * DH, D), jnp.float32) * scale, 'w_out': jax.random.normal(ks[7], (D, H * DH), jnp.float32) * scale}
    _L0_xattn_all = _L0_xattn_setup()
    _L0_xattn_in = {k: v for k, v in _L0_xattn_all.items() if k in ('position_bias', 'ln_weight', 'w_q', 'w_k', 'w_v', 'w_out')}
    del _L0_xattn_all

    def _L0_ffn_setup():
        import jax, jax.numpy as jnp
        import numpy as np
        D_MODEL = 512
        D_FF = 4 * D_MODEL
        B, S = (2, 256)
        key = jax.random.key(seed)
        kx, k1, kb1, k2, kb2 = jax.random.split(key, 5)
        s1 = 1.0 / np.sqrt(D_MODEL)
        s2 = 1.0 / np.sqrt(D_FF)
        return {'x': jax.random.normal(kx, (B, S, D_MODEL), dtype=jnp.float32), 'W1': jax.random.normal(k1, (D_MODEL, D_FF), dtype=jnp.float32) * s1, 'b1': jax.random.normal(kb1, (D_FF,), dtype=jnp.float32) * 0.01, 'W2': jax.random.normal(k2, (D_FF, D_MODEL), dtype=jnp.float32) * s2, 'b2': jax.random.normal(kb2, (D_MODEL,), dtype=jnp.float32) * 0.01}
    _L0_ffn_all = _L0_ffn_setup()
    _L0_ffn_in = {k: v for k, v in _L0_ffn_all.items() if k in ('W1', 'b1', 'W2', 'b2')}
    del _L0_ffn_all
    return {'x': x, 'ctx_4096': ctx_4096, 'mask_BxSxS2_bk0': mask_BxSxS2_bk0, 'L0_attn_freqs_cos': _L0_attn_in['freqs_cos'], 'L0_attn_freqs_sin': _L0_attn_in['freqs_sin'], 'L0_attn_wq': _L0_attn_in['wq'], 'L0_attn_wk': _L0_attn_in['wk'], 'L0_attn_wv': _L0_attn_in['wv'], 'L0_attn_wo': _L0_attn_in['wo'], 'L0_attn_k_cache': _L0_attn_in['k_cache'], 'L0_attn_v_cache': _L0_attn_in['v_cache'], 'L0_attn_block_idx': _L0_attn_in['block_idx'], 'L0_xattn_position_bias': _L0_xattn_in['position_bias'], 'L0_xattn_ln_weight': _L0_xattn_in['ln_weight'], 'L0_xattn_w_q': _L0_xattn_in['w_q'], 'L0_xattn_w_k': _L0_xattn_in['w_k'], 'L0_xattn_w_v': _L0_xattn_in['w_v'], 'L0_xattn_w_out': _L0_xattn_in['w_out'], 'L0_ffn_W1': _L0_ffn_in['W1'], 'L0_ffn_b1': _L0_ffn_in['b1'], 'L0_ffn_W2': _L0_ffn_in['W2'], 'L0_ffn_b2': _L0_ffn_in['b2']}

def reference(x, ctx_4096, mask_BxSxS2_bk0, L0_attn_freqs_cos, L0_attn_freqs_sin, L0_attn_wq, L0_attn_wk, L0_attn_wv, L0_attn_wo, L0_attn_k_cache, L0_attn_v_cache, L0_attn_block_idx, L0_xattn_position_bias, L0_xattn_ln_weight, L0_xattn_w_q, L0_xattn_w_k, L0_xattn_w_v, L0_xattn_w_out, L0_ffn_W1, L0_ffn_b1, L0_ffn_W2, L0_ffn_b2):
    import jax
    import jax.numpy as jnp

    def _L0_attn_ref(x, freqs_cos, freqs_sin, wq, wk, wv, wo, k_cache, v_cache, block_idx):
        import jax, jax.numpy as jnp
        import numpy as np
        import math
        DIM, NH, NKV, HD = (512, 32, 8, 128)
        BLOCK, NBLK, TOPK = (32, 128, 16)

        def apply_rope(x, cos, sin):
            b, l, h, d = x.shape
            xr = x.reshape(b, l, h, d // 2, 2)
            xe, xo = (xr[..., 0], xr[..., 1])
            c = cos[None, :, None, :]
            s = sin[None, :, None, :]
            oe = xe * c - xo * s
            oo = xe * s + xo * c
            return jnp.stack([oe, oo], axis=-1).reshape(b, l, h, d)
        b, l, _ = x.shape
        n_rep = NH // NKV
        q = (x @ wq.T).reshape(b, l, NH, HD)
        k = (x @ wk.T).reshape(b, l, NKV, HD)
        v = (x @ wv.T).reshape(b, l, NKV, HD)
        q = apply_rope(q, freqs_cos, freqs_sin)
        k = apply_rope(k, freqs_cos, freqs_sin)
        k_sel = k_cache[block_idx].reshape(-1, NKV, HD)
        v_sel = v_cache[block_idx].reshape(-1, NKV, HD)
        k_full = jnp.concatenate([k_sel, k[0]], axis=0)
        v_full = jnp.concatenate([v_sel, v[0]], axis=0)
        k_full = jnp.repeat(k_full.transpose(1, 0, 2)[None], n_rep, axis=1)
        v_full = jnp.repeat(v_full.transpose(1, 0, 2)[None], n_rep, axis=1)
        qh = q.transpose(0, 2, 1, 3)
        scores = jnp.einsum('bhld,bhtd->bhlt', qh, k_full) / math.sqrt(HD)
        attn = jax.nn.softmax(scores, axis=-1)
        out = jnp.einsum('bhlt,bhtd->bhld', attn, v_full)
        out = out.transpose(0, 2, 1, 3).reshape(b, l, NH * HD)
        return out @ wo.T

    def _L0_xattn_ref(hidden_states, key_value_states, attention_mask, position_bias, ln_weight, w_q, w_k, w_v, w_out):
        import jax, jax.numpy as jnp
        import numpy as np
        B, LQ, LK, D, H, DH = (2, 128, 128, 512, 32, 128)
        EPS = 1e-05

        def _rmsnorm(x, weight):
            var = jnp.mean(jnp.square(x), axis=-1, keepdims=True)
            return x * jax.lax.rsqrt(var + EPS) * weight
        x = _rmsnorm(hidden_states, ln_weight)
        b, lq, _ = x.shape
        lk = key_value_states.shape[1]
        h_q = (x @ w_q.T).reshape(b, lq, H, DH)
        h_k = (key_value_states @ w_k.T).reshape(b, lk, H, DH)
        h_v = (key_value_states @ w_v.T).reshape(b, lk, H, DH)
        score = jnp.einsum('bqhd,bkhd->bhqk', h_q, h_k)
        score = score + position_bias[None]
        m = attention_mask[:, None]
        score = jnp.where(m, score, -jnp.inf)
        score = jax.nn.softmax(score, axis=-1)
        score = jnp.where(m, score, 0.0)
        attn = jnp.einsum('bhqk,bkhd->bqhd', score, h_v).reshape(b, lq, H * DH)
        out = attn @ w_out.T
        return hidden_states + out

    def _L0_ffn_ref(x, W1, b1, W2, b2):
        import jax, jax.numpy as jnp
        import numpy as np
        D_MODEL = 512
        D_FF = 4 * D_MODEL
        B, S = (2, 256)
        orig_shape = x.shape
        flat_x = x.reshape(-1, D_MODEL)
        h = jax.nn.gelu(flat_x @ W1 + b1)
        y = h @ W2
        y = jnp.nan_to_num(y, nan=0.0, posinf=0.0, neginf=0.0)
        return y.reshape(orig_shape) + b2
    x = x + _L0_attn_ref(_layernorm(x, axis=-1), L0_attn_freqs_cos, L0_attn_freqs_sin, L0_attn_wq, L0_attn_wk, L0_attn_wv, L0_attn_wo, L0_attn_k_cache, L0_attn_v_cache, L0_attn_block_idx)
    x = x + _L0_xattn_ref(_layernorm(x, axis=-1), ctx_4096, mask_BxSxS2_bk0, L0_xattn_position_bias, L0_xattn_ln_weight, L0_xattn_w_q, L0_xattn_w_k, L0_xattn_w_v, L0_xattn_w_out)
    x = x + _L0_ffn_ref(_layernorm(x, axis=-1), L0_ffn_W1, L0_ffn_b1, L0_ffn_W2, L0_ffn_b2)
    return x

_drawn_inputs = setup_inputs


def setup_inputs(seed=0):
    import zlib

    import numpy as np

    out = dict(_drawn_inputs(seed))
    spreads = {'L0_xattn_ln_weight': (1.0, 0.6)}
    factors = {'L0_attn_freqs_cos': 2.672,
     'L0_attn_freqs_sin': 3.798,
     'L0_attn_wk': 8.0,
     'L0_attn_wv': 5.979,
     'L0_ffn_b1': 36.181,
     'L0_ffn_b2': 25.298,
     'L0_attn_k_cache': 8.0,
     'L0_attn_v_cache': 8.0}
    for name, (base, spread) in spreads.items():
        noise = np.random.default_rng([zlib.crc32(name.encode()), seed]).standard_normal(out[name].shape)
        drawn = base * np.exp(spread * noise) if base else spread * noise
        out[name] = jnp.asarray(drawn.astype(out[name].dtype))
    for name, factor in factors.items():
        out[name] = (out[name] * factor).astype(out[name].dtype)
    return out
```

```python
from contextlib import ExitStack

import concourse.bass as bass
from concourse import mybir

F32 = mybir.dt.float32
F32R = mybir.dt.float32r
U8 = mybir.dt.uint8
I32 = mybir.dt.int32
ALU = mybir.AluOpType
ACT = mybir.ActivationFunctionType
AX_X = mybir.AxisListType.X

P = 128
B, D = 8, 512
C = D // P
TOK = B * P
HALF = TOK // 2
NH, NKV = 32, 8
REP = NH // NKV
TOPK, BLOCK, NBLK = 16, 32, 128
T = TOPK * BLOCK + P
KT = T // P
KB = T // BLOCK
TH = T // 2
FF = 4 * D
NF = FF // P
UNITS = 2 * NH
FUNITS = 2 * NF
SCALE = float(P) ** -0.5
EPS = 1e-5
NEG = -1e30


def decoder_layer(nc, x, ctxT, mask, fcos, fsin, wq, wk, wv, wo, kc, vc, bidx,
                  xbias, lnw, xwq, xwk, xwv, xwo, w1, b1, w2, b2, out):
    with ExitStack() as ctx:
        def sb(stack, name, shape, dt=F32):
            return stack.enter_context(nc.sbuf_tensor(name, shape, dt))

        def pair(stack, name, shape):
            return sb(stack, name + "_hi", shape, F32R), sb(stack, name + "_lo", shape, F32R)

        def sem(name):
            return ctx.enter_context(nc.semaphore(name))

        xacc = sb(ctx, "xacc", [P, B, D])
        xT_hi, xT_lo = pair(ctx, "xT", [P, C, TOK])
        ident = sb(ctx, "ident", [P, P])
        stats = sb(ctx, "stats", [P, B, 6])
        meanvar = sb(ctx, "meanvar", [P, B, 2])
        nrm = sb(ctx, "nrm", [P, 10, B])
        negmax = sb(ctx, "negmax", [P, 2, 4])
        rowsum = sb(ctx, "rowsum", [P, 2, 4])
        rinv = sb(ctx, "rinv", [P, 2, 4])

        with ExitStack() as ph:
            K_all = sb(ph, "K_all", [P, KB, NKV, BLOCK])
            V_all = sb(ph, "V_all", [P, KT, NKV * P])
            K_hi, K_lo = pair(ph, "K", [P, 2, T])
            q_hi, q_lo = pair(ph, "q", [P, 2, HALF])
            wq_raw = sb(ph, "wq_raw", [P, 2, C, P])
            wq_cos = sb(ph, "wq_cos", [P, C, P])
            wq_sin = sb(ph, "wq_sin", [P, C, P])
            wq_rot = sb(ph, "wq_rot", [P, C, P])
            wq_hi, wq_lo = pair(ph, "wq", [P, 2, C, P])
            V_hi, V_lo = pair(ph, "V", [P, 2, KT, P])
            wo_raw = sb(ph, "wo_raw", [P, 2, D])
            wo_hi, wo_lo = pair(ph, "wo", [P, 2, D])
            rope = sb(ph, "rope", [P, 2, P])
            ropeq = sb(ph, "ropeq", [P, 2, P])
            idx_sb = sb(ph, "idx_sb", [1, TOPK], I32)
            with ExitStack() as pro:
                kv_raw = sb(pro, "kv_raw", [P, 2, C, D])
                knew = sb(pro, "knew", [P, 3, D])
                kv_stage = [pair(pro, "kv0", [P, C, D]), None]
                with ExitStack() as pro2:
                    xn1 = sb(pro2, "xn1", [P, B, D])
                with ExitStack() as pro2:
                    kv_stage[1] = pair(pro2, "kv1", [P, C, D])
            with ExitStack() as lo_:
                prob = sb(lo_, "prob", [P, 2, 4, T])
                pT_hi, pT_lo = pair(lo_, "pT", [P, KT, HALF])
                oT_hi, oT_lo = pair(lo_, "oT", [P, HALF])
                xwv_raw = sb(lo_, "xwv_raw", [P, C, 2 * P])
                xwv_hi, xwv_lo = pair(lo_, "xwv", [P, C, 2 * P])
        with ExitStack() as ph:
            cT_hi, cT_lo = pair(ph, "cT", [P, C, TOK])
            c_raw = sb(ph, "c_raw", [P, 2, TOK])
            xwk_raw = sb(ph, "xwk_raw", [P, 2, C, P])
            xwk_hi, xwk_lo = pair(ph, "xwk", [P, 2, C, P])
            xwq_raw = sb(ph, "xwq_raw", [P, 2, C, P])
            xwq_hi, xwq_lo = pair(ph, "xwq", [P, 2, C, P])
            bias_sb = sb(ph, "bias_sb", [P, 2, P])
            mask_sb = sb(ph, "mask_sb", [P, B, P], U8)
            negmask = sb(ph, "negmask", [P, B, P])
            lnw_sb = sb(ph, "lnw_sb", [P, D])
            xwo_raw = sb(ph, "xwo_raw", [P, 2, D])
            xwo_hi, xwo_lo = pair(ph, "xwo", [P, 2, D])
            anykey = sb(ph, "anykey", [P, B])
            comb = sb(ph, "comb", [P, 2, 4, P])
            xq_hi, xq_lo = pair(ph, "xq", [P, 2, HALF])
            xk = sb(ph, "xk", [P, 2, 4, 2, P], F32R)
            xV_hi, xV_lo = pair(ph, "xV", [P, 2, 4, 2 * P])
            with ExitStack() as pro:
                xn2 = sb(pro, "xn2", [P, B, D])
            with ExitStack() as lo_:
                xprob = sb(lo_, "xprob", [P, 2, 4, P])
                xscore = sb(lo_, "xscore", [P, 2, 4, P])
                xpT = sb(lo_, "xpT", [P, 4, 2, P], F32R)
                xo = sb(lo_, "xo", [P, 2, 4, P])
                xoT_hi, xoT_lo = pair(lo_, "xoT", [P, 2, HALF])
        with ExitStack() as ph:
            w1_raw = sb(ph, "w1_raw", [P, 2, C, P])
            w1_hi, w1_lo = pair(ph, "w1", [P, 2, C, P])
            w2_raw = sb(ph, "w2_raw", [P, 2, D])
            w2_hi, w2_lo = pair(ph, "w2", [P, 2, D])
            b1_sb = sb(ph, "b1_sb", [P, 2])
            b2_sb = sb(ph, "b2_sb", [P, D])
            hid = sb(ph, "hid", [P, 2, HALF])
            hid_hi, hid_lo = pair(ph, "hid", [P, 2, HALF])
            xn3 = sb(ph, "xn3", [P, B, D])
            yacc = sb(ph, "yacc", [P, B, D])
            finite = sb(ph, "finite", [P, B, D], I32)
            ysum = sb(ph, "ysum", [P, B, D])

        bank = ctx.enter_context(nc.psum_tensor("bank", [P, 8, 512], F32))

        s_x = [sem(f"x_in{b}") for b in range(B)]
        s_rope_in, s_idx_in = sem("rope_in"), sem("idx_in")
        s_kcache, s_vcache = sem("kcache_in"), sem("vcache_in")
        s_kvraw = [sem(f"kvraw_in{i}") for i in range(2)]
        s_ident = sem("ident_made")
        s_dve, s_pool = sem("dve_chain"), sem("pool_chain")
        L = {}
        for p in (1, 2, 3):
            for e in ("stat", "sqrt", "xn", "tr", "hi", "lo"):
                L[p, e] = sem(f"ln{p}_{e}")
        s_rope = sem("rope_made")
        s_kvhi, s_kvlo, s_kvmm, s_knew, s_ktr, s_kvev = (sem(n) for n in (
            "kv_hi_made", "kv_lo_made", "kv_product", "knew_roped", "knew_transposed", "kv_evacuated"))
        s_wqraw = [sem(f"wqraw_in{i}") for i in range(2)]
        s_woraw = [sem(f"woraw_in{i}") for i in range(2)]
        s_xl, s_factor = sem("centred_weighted"), sem("factors_made")
        a_rot1, c_r1, c_s1 = sem("a_rot_products"), sem("c_reciprocal"), sem("c_score_hi")
        a = {n: sem("a_" + n) for n in (
            "Khi", "Klo", "Vhi", "Vlo", "rot", "wqhi", "wqlo", "wohi", "wolo", "S", "max", "exp", "tr",
            "pThi", "pTlo", "pv", "oThi", "oTlo", "q", "qhi", "qlo", "rinv", "wo", "y")}
        s_ctx, s_mask, s_lnw = [sem(f"ctx_in{i}") for i in range(2)], sem("mask_in"), sem("lnw_in")
        s_y0, s_xb = sem("yacc_cleared"), sem("residual_and_bias")
        s_chi, s_clo, s_neg, s_any = sem("ctx_hi_made"), sem("ctx_lo_made"), sem("negmask_made"), sem("anykey_made")
        s_xraw = {n: [sem(f"x{n}raw_in{i}") for i in range(2)] for n in ("q", "k", "o", "bias")}
        s_xvraw = sem("xvraw_in")
        c = {n: sem("c_" + n) for n in (
            "qwhi", "qwlo", "kwhi", "kwlo", "vwhi", "vwlo", "owhi", "owlo", "comb", "S", "score", "max", "exp",
            "tr", "pThi", "pTlo", "pv", "ohi", "osum", "oThi", "oTlo", "q", "qhi", "qlo", "k", "khi", "klo", "v", "vhi", "vlo",
            "rinv", "wo", "y", "res")}
        s_w1raw = [sem(f"w1raw_in{i}") for i in range(2)]
        s_w2raw = [sem(f"w2raw_in{i}") for i in range(2)]
        s_b = sem("b2_in")
        s_b1 = [sem(f"b1_in{i}") for i in range(2)]
        f = {n: sem("f_" + n) for n in (
            "w1hi", "w1lo", "w2hi", "w2lo", "h", "gelu", "hhi", "hlo", "y", "acc", "sum", "finite", "fin")}
        s_out = sem("out_written")

        S_bank = [bank[:, 2 * i:2 * i + 2, 0:TH] for i in range(2)]
        T_bank = [bank[:, 4 + i, :] for i in range(2)]
        O_bank, M_bank = bank[:, 6, :], bank[:, 7, :]
        XS_bank = bank[:, 0:2, :].rearrange("p b (t n) -> p (b t) n", t=2)
        XO_bank = bank[:, 2:4, :].rearrange("p b (t n) -> p (b t) n", t=2)
        XT_bank, XQ_bank, XK_bank, XV_bank = (bank[:, i, :] for i in (2, 4, 5, 6))
        XW_last = [bank[:, i, :] for i in (7, 5, 6, 4)]
        XW_bank = [bank[:, i, :] for i in (7, 7, 7, 4)]
        H_bank = [bank[:, i, :] for i in range(2)]
        Y_bank = [bank[:, 2 + i, :] for i in range(4)]

        def ln_bank(p, b):
            return b if p == 3 else b % 4

        LAST1 = 4 * UNITS
        block = ctx.enter_context(nc.Block())

        @block.sync
        def _(sp):
            sp.dma_start(rope[:, 0, 0:64], fcos.partition_broadcast(P)).then_inc(s_rope_in, 16)
            sp.dma_start(rope[:, 1, 0:64], fsin.partition_broadcast(P)).then_inc(s_rope_in, 16)
            sp.dma_start(idx_sb[:, :], bidx).then_inc(s_idx_in, 16)
            for b in range(4):
                sp.dma_start(xacc[:, b, :], x[b]).then_inc(s_x[b], 16)
            for h in range(2):
                sp.dma_start(wq_raw[:, h], wq[h]).then_inc(s_wqraw[h], 16)
            for b in range(4, B):
                sp.dma_start(xacc[:, b, :], x[b]).then_inc(s_x[b], 16)
            kv_src = [wk[0], wk[1], wv[0], wv[1]]
            sp.dma_start(kv_raw[:, 0], kv_src[0]).then_inc(s_kvraw[0], 16)
            sp.dma_start(kv_raw[:, 1], kv_src[1]).then_inc(s_kvraw[1], 16)
            sp.wait_ge(s_idx_in, 16)
            for t in range(TOPK):
                blk = sp.value_load(idx_sb[0:1, t:t + 1], min_val=0, max_val=NBLK - 1)
                sp.dma_start(K_all[:, t], kc[bass.ds(blk, 1)].rearrange("a d g t -> (a d) g t"))\
                  .then_inc(s_kcache, 16)
                r = BLOCK * (t % (P // BLOCK))
                sp.dma_start(V_all[r:r + BLOCK, t // (P // BLOCK), :],
                             vc[bass.ds(blk, 1)].rearrange("a t n -> (a t) n")).then_inc(s_vcache, 16)
            for m in range(2, 4):
                sp.wait_ge(s_kvhi, m - 1)
                sp.wait_ge(s_kvlo, m - 1)
                sp.dma_start(kv_raw[:, m % 2], kv_src[m]).then_inc(s_kvraw[m % 2], 16)
            for h in range(2):
                sp.dma_start(wo_raw[:, h], wo[h]).then_inc(s_woraw[h], 16)
            sp.wait_ge(a["rot"], 1)
            sp.dma_start(wq_raw[:, 0], wq[2]).then_inc(s_wqraw[0], 16)

            def a_load(it, u):
                if u % 2:
                    return
                h, hp = it * 4 + u // 2, (u // 2) % 2
                if not isinstance(h, int) or h + 3 < NH:
                    sp.wait_ge(a["rot"], h + 2)
                    sp.dma_start(wq_raw[:, (hp + 1) % 2],
                                 wq[bass.ds(h + 3, 1)].rearrange("a p c n -> (a p) c n"))\
                      .then_inc(s_wqraw[(hp + 1) % 2], 16)
                if not isinstance(h, int) or h + 2 < NH:
                    sp.wait_ge(a["wohi"], h + 1)
                    sp.wait_ge(a["wolo"], h + 1)
                    sp.dma_start(wo_raw[:, hp], wo[bass.ds(h + 2, 1)].rearrange("a p n -> (a p) n"))\
                      .then_inc(s_woraw[hp], 16)

            a_load(0, 0)
            with sp.Fori(0, 7) as it:
                for u in range(1, 9):
                    a_load(it, u)
            for u in range(1, 8):
                a_load(7, u)

            for ch in range(C):
                if ch == 0:
                    sp.wait_ge(a["Vlo"], NH // 2)
                    sp.dma_start(xwv_raw[:, :, :], xwv[0]).then_inc(s_xvraw, 16)
                elif ch >= 2:
                    sp.wait_ge(s_clo, ch - 1)
                sp.dma_start(c_raw[:, ch % 2, :], ctxT[:, ch, :]).then_inc(s_ctx[ch % 2], 16)
            sp.wait_ge(a["S"], LAST1)
            sp.dma_start(xwk_raw[:, 0], xwk[0]).then_inc(s_xraw["k"][0], 16)
            sp.dma_start(xwq_raw[:, 0], xwq[0]).then_inc(s_xraw["q"][0], 16)
            sp.dma_start(mask_sb[:, :, :], mask).then_inc(s_mask, 16)
            sp.dma_start(lnw_sb[:, :], lnw.partition_broadcast(P)).then_inc(s_lnw, 16)
            for h in range(2):
                sp.dma_start(bias_sb[:, h], xbias[h]).then_inc(s_xraw["bias"][h], 16)
            sp.dma_start(xwk_raw[:, 1], xwk[1]).then_inc(s_xraw["k"][1], 16)
            sp.dma_start(xwq_raw[:, 1], xwq[1]).then_inc(s_xraw["q"][1], 16)
            sp.wait_ge(a["wo"], LAST1)
            for h in range(2):
                sp.dma_start(xwo_raw[:, h], xwo[h]).then_inc(s_xraw["o"][h], 16)
            sp.wait_ge(c["vwhi"], 1)
            sp.wait_ge(c["vwlo"], 1)
            sp.dma_start(xwv_raw[:, :, :], xwv[1]).then_inc(s_xvraw, 16)

            def c_load(it, u):
                if u % 2:
                    return
                h, hp = it * 2 + u // 2, (u // 2) % 2
                static = isinstance(h, int)
                if not static or h + 2 < NH:
                    for n, raw, src in (("q", xwq_raw, xwq), ("k", xwk_raw, xwk), ("o", xwo_raw, xwo)):
                        sp.wait_ge(c[n + "whi"], h + 1)
                        sp.wait_ge(c[n + "wlo"], h + 1)
                        src2 = src[bass.ds(h + 2, 1)]
                        src2 = src2.rearrange("a p c n -> (a p) c n") if n != "o" else src2.rearrange("a p n -> (a p) n")
                        sp.dma_start(raw[:, hp], src2).then_inc(s_xraw[n][hp], 16)
                    sp.wait_ge(c["comb"], 2 * h + 2)
                    sp.dma_start(bias_sb[:, hp], xbias[bass.ds(h + 2, 1)].rearrange("a p n -> (a p) n"))\
                      .then_inc(s_xraw["bias"][hp], 16)
                if u % 4 == 2 and (not static or h // 2 + 2 < NH // 2):
                    pr = it + u // 4
                    sp.wait_ge(c["vwhi"], pr + 2)
                    sp.wait_ge(c["vwlo"], pr + 2)
                    sp.dma_start(xwv_raw[:, :, :], xwv[bass.ds(pr + 2, 1)].rearrange("a p c n -> (a p) c n"))\
                      .then_inc(s_xvraw, 16)

            c_load(0, 0)
            with sp.Fori(0, 14) as it:
                for u in range(1, 5):
                    c_load(it, u)
            for u in range(1, 8):
                c_load(14, u)

            sp.wait_ge(c["k"], UNITS)
            sp.dma_start(b2_sb[:, :], b2.partition_broadcast(P)).then_inc(s_b, 16)
            for h in range(2):
                sp.dma_start(w1_raw[:, h], w1[h]).then_inc(s_w1raw[h], 16)
                sp.dma_start(w2_raw[:, h], w2[h]).then_inc(s_w2raw[h], 16)
                sp.dma_start(b1_sb[:, h:h + 1], b1[h]).then_inc(s_b1[h], 16)

            def f_load(it, u):
                if u % 2:
                    return
                h, hp = it * 2 + u // 2, (u // 2) % 2
                if not isinstance(h, int) or h + 2 < NF:
                    sp.wait_ge(f["w1hi"], h + 1)
                    sp.wait_ge(f["w1lo"], h + 1)
                    sp.dma_start(w1_raw[:, hp], w1[bass.ds(h + 2, 1)].rearrange("a p c n -> (a p) c n"))\
                      .then_inc(s_w1raw[hp], 16)
                    sp.wait_ge(f["w2hi"], h + 1)
                    sp.wait_ge(f["w2lo"], h + 1)
                    sp.dma_start(w2_raw[:, hp], w2[bass.ds(h + 2, 1)].rearrange("a p n -> (a p) n"))\
                      .then_inc(s_w2raw[hp], 16)
                    sp.wait_ge(f["gelu"], 2 * h + 2)
                    sp.dma_start(b1_sb[:, hp:hp + 1], b1[bass.ds(h + 2, 1)].rearrange("a p n -> (a p) n"))\
                      .then_inc(s_b1[hp], 16)

            f_load(0, 0)
            with sp.Fori(0, 6) as it:
                for u in range(1, 5):
                    f_load(it, u)
            for u in range(1, 8):
                f_load(6, u)
            for b in range(B):
                sp.wait_ge(f["fin"], b + 1)
                sp.dma_start(out[b], xacc[:, b, :]).then_inc(s_out, 16)
            sp.wait_ge(s_out, 16 * B)

        @block.gpsimd
        def _(pool):
            g = nc.gpsimd
            chain = [0]

            def link(ins):
                chain[0] += 1
                ins.then_inc(s_pool, 1)
                pool.wait_ge(s_pool, chain[0])

            link(g.memset(ident[:, :], 0.0))
            g.affine_select(out=ident[:, :], in_=ident[:, :], compare_op=ALU.not_equal, fill=1.0, base=0,
                            pattern=[[-1, P]], channel_multiplier=1).then_inc(s_ident, 1)

            def rotate(h, hp, loads):
                pool.wait_ge(s_wqraw[hp], loads)
                if h is not None:
                    pool.wait_ge(a["wqhi"], h)
                    pool.wait_ge(a["wqlo"], h)
                cos = ropeq[:, 0, :].unsqueeze(1).to_broadcast([P, C, P])
                src = wq_raw[:, hp]
                half = P // 2
                g.tensor_tensor(wq_cos[:, :, :], src, cos, ALU.mult)
                for e in range(2):
                    s_ = ropeq[:, 1, e * half:(e + 1) * half].unsqueeze(1).to_broadcast([P, C, half])
                    last = g.tensor_tensor(wq_sin[:, :, e * half:(e + 1) * half],
                                           src[:, :, (1 - e) * half:(2 - e) * half], s_, ALU.mult)
                return last

            def split_wq(h, hp, loads, first=False):
                rotate(None if first else h, hp, loads).then_inc(a_rot1, 1)
                pool.wait_ge(a_rot1, h + 1)
                g.tensor_tensor(wq_rot[:, :, :], wq_cos[:, :, :], wq_sin[:, :, :], ALU.add).then_inc(a["rot"], 1)
                pool.wait_ge(a["wqhi"], h + 1)
                pool.wait_ge(a["rot"], h + 1)
                g.tensor_tensor(wq_lo[:, hp], wq_rot[:, :, :], wq_hi[:, hp], ALU.subtract).then_inc(a["wqlo"], 1)

            def split_lo(dst, raw, hi, hi_sem, h, lo_sem):
                pool.wait_ge(hi_sem, h + 1)
                g.tensor_tensor(dst, raw, hi, ALU.subtract).then_inc(lo_sem, 1)

            pool.wait_ge(s_rope, 1)
            for h in range(2):
                split_wq(h, h, 16, first=(h == 0))
            split_lo(wo_lo[:, 0], wo_raw[:, 0], wo_hi[:, 0], a["wohi"], 0, a["wolo"])

            def a_step(it, u):
                h, hp = it * 4 + u // 2, (u // 2) % 2
                if u % 2 == 0 and (not isinstance(h, int) or h + 2 < NH):
                    split_wq(h + 2, hp, (it * 2 + u // 4 + 2) * 16)
                if u % 2 == 1 and (not isinstance(h, int) or h + 1 < NH):
                    split_lo(wo_lo[:, 1 - hp], wo_raw[:, 1 - hp], wo_hi[:, 1 - hp], a["wohi"], h + 1, a["wolo"])
                if isinstance(h, int) and UNITS - 6 <= it * 8 + u < UNITS - 2:
                    ch = it * 8 + u - (UNITS - 6)
                    split_lo(cT_lo[:, ch, :], c_raw[:, ch % 2, :], cT_hi[:, ch, :], s_chi, ch, s_clo)

            a_step(0, 0)
            with pool.Fori(0, 7) as it:
                for u in range(1, 9):
                    a_step(it, u)
            for u in range(1, 8):
                a_step(7, u)

            split_lo(xwv_lo[:, :, :], xwv_raw[:, :, :], xwv_hi[:, :, :], c["vwhi"], 0, c["vwlo"])
            for h in range(2):
                split_lo(xwk_lo[:, h], xwk_raw[:, h], xwk_hi[:, h], c["kwhi"], h, c["kwlo"])
                split_lo(xwq_lo[:, h], xwq_raw[:, h], xwq_hi[:, h], c["qwhi"], h, c["qwlo"])
            pool.wait_ge(s_mask, 16)
            g.tensor_scalar(negmask[:, :, :], mask_sb[:, :, :], -NEG, NEG, ALU.mult, ALU.add).then_inc(s_neg, 1)

            def bias_mask(n, half, hp, loads):
                pool.wait_ge(s_xraw["bias"][hp], loads)
                g.tensor_tensor(comb[:, half], bias_sb[:, hp].unsqueeze(1).to_broadcast([P, 4, P]),
                                negmask[:, 4 * half:4 * half + 4, :], ALU.add).then_inc(c["comb"], 1)

            pool.wait_ge(s_neg, 1)
            pool.wait_ge(a["wo"], LAST1)
            for n in range(2):
                bias_mask(n, n, 0, 16)
            split_lo(xwo_lo[:, 0], xwo_raw[:, 0], xwo_hi[:, 0], c["owhi"], 0, c["owlo"])

            def c_step(it, u):
                n = it * 4 + u
                h, hp = it * 2 + u // 2, (u // 2) % 2
                static = isinstance(h, int)
                if not static or n + 2 < UNITS:
                    pool.wait_ge(c["score"], n + 1)
                    bias_mask(n + 2, u % 2, 1 - hp, (it + (u // 2 + 1) // 2 + 1) * 16)
                if u % 2 == 0 and (not static or h + 2 < NH):
                    split_lo(xwq_lo[:, hp], xwq_raw[:, hp], xwq_hi[:, hp], c["qwhi"], h + 2, c["qwlo"])
                    split_lo(xwk_lo[:, hp], xwk_raw[:, hp], xwk_hi[:, hp], c["kwhi"], h + 2, c["kwlo"])
                if u % 2 == 1 and (not static or h + 1 < NH):
                    split_lo(xwo_lo[:, 1 - hp], xwo_raw[:, 1 - hp], xwo_hi[:, 1 - hp], c["owhi"], h + 1, c["owlo"])
                if u % 4 == 1 and (not static or it + u // 4 + 1 < NH // 2):
                    split_lo(xwv_lo[:, :, :], xwv_raw[:, :, :], xwv_hi[:, :, :], c["vwhi"], it + u // 4 + 1, c["vwlo"])

            c_step(0, 0)
            with pool.Fori(0, 14) as it:
                for u in range(1, 5):
                    c_step(it, u)
            for u in range(1, 8):
                c_step(14, u)

            for h in range(2):
                split_lo(w1_lo[:, h], w1_raw[:, h], w1_hi[:, h], f["w1hi"], h, f["w1lo"])
            split_lo(w2_lo[:, 0], w2_raw[:, 0], w2_hi[:, 0], f["w2hi"], 0, f["w2lo"])
            pool.wait_ge(c["wo"], LAST1)
            g.memset(yacc[:, :, :], 0.0).then_inc(s_y0, 1)
            pool.wait_ge(s_b, 16)
            for b in range(B):
                pool.wait_ge(L[3, "xn"], b + 1)
                g.tensor_tensor(xacc[:, b, :], xacc[:, b, :], b2_sb[:, :], ALU.add).then_inc(s_xb, 1)

            def f_step(it, u):
                h, hp = it * 2 + u // 2, (u // 2) % 2
                static = isinstance(h, int)
                if u % 2 == 0 and (not static or h + 2 < NF):
                    split_lo(w1_lo[:, hp], w1_raw[:, hp], w1_hi[:, hp], f["w1hi"], h + 2, f["w1lo"])
                if u % 2 == 1 and (not static or h + 1 < NF):
                    split_lo(w2_lo[:, 1 - hp], w2_raw[:, 1 - hp], w2_hi[:, 1 - hp], f["w2hi"], h + 1, f["w2lo"])

            f_step(0, 0)
            with pool.Fori(0, 6) as it:
                for u in range(1, 5):
                    f_step(it, u)
            for u in range(1, 8):
                f_step(6, u)
            for b in range(B):
                pool.wait_ge(f["acc"], 4 * FUNITS - (4 if b < 4 else 0) - 3 + b % 4)
                if b == 0:
                    pool.wait_ge(s_xb, B)
                g.tensor_tensor(ysum[:, b, :], yacc[:, b, :], xacc[:, b, :], ALU.add).then_inc(f["sum"], 1)

        @block.scalar
        def _(act):
            s = nc.scalar

            def copy(dst, src):
                return s.activation(dst, src, ACT.Copy)

            def ln_sqrt(p, cnt):
                tiles = slice(4 * ((cnt - 1) // (2 if p == 2 else 1)), 4 * ((cnt - 1) // (2 if p == 2 else 1)) + 4)
                act.wait_ge(L[p, "stat"], cnt)
                s.activation(nrm[:, 1, tiles], nrm[:, 0, tiles], ACT.Sqrt).then_inc(L[p, "sqrt"], 1)

            def ln_hi(p, half):
                for b in range(4 * half, 4 * half + 4):
                    act.wait_ge(L[p, "tr"], b + 1)
                    copy(xT_hi[:, :, b * P:(b + 1) * P],
                         bank[:, ln_bank(p, b), :].rearrange("p (c n) -> p c n", c=C)).then_inc(L[p, "hi"], 1)

            def ln_scale(half):
                for b in range(4 * half, 4 * half + 4):
                    act.wait_ge(s_xl, b + 1)
                    act.wait_ge(s_factor, half + 1)
                    s.activation(xn2[:, b, :], xn2[:, b, :], ACT.Copy, scale=nrm[:, 6, b:b + 1])\
                     .then_inc(L[2, "xn"], 1)

            def kv_split(m):
                act.wait_ge(s_kvraw[m % 2], 16 * (m // 2 + 1))
                if m >= 2:
                    act.wait_ge(s_kvmm, m - 1)
                copy(kv_stage[m % 2][0][:, :, :], kv_raw[:, m % 2]).then_inc(s_kvhi, 1)

            def kv_evac(m):
                if m < 2:
                    act.wait_ge(s_ktr, m + 1)
                    for g_ in range(4):
                        last = copy(K_all[:, TOPK:KB, 4 * m + g_, :],
                                    bank[:, 6, g_ * P:(g_ + 1) * P].rearrange("p (b t) -> p b t", t=BLOCK))
                else:
                    act.wait_ge(s_kvmm, m + 1)
                    last = copy(V_all[:, KT - 1, (m - 2) * D:(m - 1) * D], bank[:, 4 + m % 2, :])
                last.then_inc(s_kvev, 1)

            def wq_split(h, hp):
                act.wait_ge(a["rot"], h + 1)
                copy(wq_hi[:, hp], wq_rot[:, :, :]).then_inc(a["wqhi"], 1)

            def raw_split(hi, raw, in_sem, loads, out_sem):
                act.wait_ge(in_sem, loads)
                copy(hi, raw).then_inc(out_sem, 1)

            def kv_group(grp, slot):
                act.wait_ge(s_kcache, 16 * TOPK)
                act.wait_ge(s_vcache, 16 * TOPK)
                copy(K_hi[:, slot].rearrange("p (b t) -> p b t", t=BLOCK), K_all[:, :, grp, :]).then_inc(a["Khi"], 1)
                copy(V_hi[:, slot], V_all[:, :, bass.ds(grp * P, P)] if not isinstance(grp, int)
                     else V_all[:, :, grp * P:(grp + 1) * P]).then_inc(a["Vhi"], 1)

            def exps(n, slot, i):
                act.wait_ge(a["max"], 4 * n + i + 1)
                s.activation(prob[:, slot, i, :].rearrange("p (a t) -> p a t", a=2), S_bank[i % 2], ACT.Exp,
                             bias=negmax[:, slot, i:i + 1], scale=1.0,
                             accum_out=rowsum[:, slot, i:i + 1]).then_inc(a["exp"], 1)

            def q_evac(n, k, cnt):
                act.wait_ge(a["q"], cnt)
                copy(q_hi[:, k], M_bank).then_inc(a["qhi"], 1)

            ln_sqrt(1, 1)
            wq_split(0, 0)
            ln_hi(1, 0)
            ln_sqrt(1, 2)
            kv_split(0)
            q_evac(0, 0, 1)
            ln_hi(1, 1)
            kv_split(1)
            q_evac(1, 1, 2)
            wq_split(1, 1)
            for m in range(2, 4):
                kv_split(m)
                kv_evac(m - 2)
            raw_split(wo_hi[:, 0], wo_raw[:, 0], s_woraw[0], 16, a["wohi"])
            kv_evac(2)
            kv_evac(3)
            act.wait_ge(s_kvev, 4)
            kv_group(0, 0)
            for i in range(4):
                exps(0, 0, i)

            def a_step(it, u):
                n, k = it * 8 + u, u % 2
                h, hp = it * 4 + u // 2, (u // 2) % 2
                static = isinstance(n, int)
                more1, more2 = (not static or n + 1 < UNITS), (not static or n + 2 < UNITS)
                if not (static and n == 0):
                    act.wait_ge(a["pv"], n)
                    copy(oT_hi[:, :], O_bank).then_inc(a["oThi"], 1)
                for j in range(KT):
                    if j == 0:
                        if more1:
                            exps(n + 1, 1 - k, 0)
                        if more2:
                            act.wait_ge(a["q"], n + 3)
                            copy(q_hi[:, k], M_bank).then_inc(a["qhi"], 1)
                    if static and n == UNITS - 1 and j == 3:
                        raw_split(xwv_hi[:, :, :], xwv_raw[:, :, :], s_xvraw, 16, c["vwhi"])
                        for h_ in range(2):
                            raw_split(xwk_hi[:, h_], xwk_raw[:, h_], s_xraw["k"][h_], 16, c["kwhi"])
                            raw_split(xwq_hi[:, h_], xwq_raw[:, h_], s_xraw["q"][h_], 16, c["qwhi"])
                    act.wait_ge(a["tr"], KT * n + j + 1)
                    copy(pT_hi[:, j, :], T_bank[j % 2 if k == 0 else (j + 1) % 2]).then_inc(a["pThi"], 1)
                    if 0 < j < 4 and more1:
                        exps(n + 1, 1 - k, j)
                if k == 0 and (not static or h + 2 < NH):
                    wq_split(h + 2, hp)
                if k == 1 and (not static or h + 1 < NH):
                    raw_split(wo_hi[:, 1 - hp], wo_raw[:, 1 - hp], s_woraw[1 - hp],
                              (it * 2 + (u // 2 + 1) // 2 + 1) * 16, a["wohi"])
                if u % 4 == 1 and (not static or n // 4 + 1 < UNITS // 4):
                    kv_group(it + (u // 4 + 1) // 2, (u // 4 + 1) % 2)
                if static and UNITS - 6 <= n < UNITS - 2:
                    ch = n - (UNITS - 6)
                    act.wait_ge(s_ctx[ch % 2], 16 * (ch // 2 + 1))
                    copy(cT_hi[:, ch, :], c_raw[:, ch % 2, :]).then_inc(s_chi, 1)

            a_step(0, 0)
            with act.Fori(0, 7) as it:
                for u in range(1, 9):
                    a_step(it, u)
            for u in range(1, 8):
                a_step(7, u)
            act.wait_ge(a["pv"], UNITS)
            copy(oT_hi[:, :], O_bank).then_inc(a["oThi"], 1)

            def k_evac(n, k, cnt):
                act.wait_ge(c["k"], cnt)
                copy(xk[:, k, :, 0, :], XK_bank.rearrange("p (t n) -> p t n", t=4)).then_inc(c["khi"], 1)

            def xq_evac(n, k, cnt):
                act.wait_ge(c["q"], cnt)
                copy(xq_hi[:, k], XQ_bank).then_inc(c["qhi"], 1)

            def c_exps(n, slot):
                for i in range(4):
                    act.wait_ge(c["max"], n + 1)
                    s.activation(xprob[:, slot, i, :], xscore[:, slot, i, :], ACT.Exp,
                                 bias=negmax[:, slot, i:i + 1], scale=1.0,
                                 accum_out=rowsum[:, slot, i:i + 1]).then_inc(c["exp"], 1)

            def residual(half):
                for b in range(4 * half, 4 * half + 4):
                    act.wait_ge(L[2, "xn"], b + 1)
                    s.activation(xacc[:, b, :], xacc[:, b, :], ACT.Identity, bias=nrm[:, 9, b:b + 1],
                                 scale=nrm[:, 8, b:b + 1]).then_inc(c["res"], 1)

            def v_evac(half, j, cnt):
                act.wait_ge(c["v"], cnt)
                copy(xV_hi[:, half, 2 * j:2 * j + 2, :],
                     XV_bank.rearrange("p (t n) -> p t n", t=2)).then_inc(c["vhi"], 1)

            ln_sqrt(2, 1)
            v_evac(0, 0, 1)
            ln_sqrt(2, 2)
            v_evac(0, 1, 2)
            ln_scale(0)
            k_evac(0, 0, 1)
            ln_hi(2, 0)
            residual(0)
            v_evac(1, 0, 3)
            ln_sqrt(2, 3)
            k_evac(1, 1, 2)
            ln_sqrt(2, 4)
            ln_scale(1)
            xq_evac(0, 0, 1)
            v_evac(1, 1, 4)
            ln_hi(2, 1)
            c_exps(0, 0)
            xq_evac(1, 1, 2)
            raw_split(xwo_hi[:, 0], xwo_raw[:, 0], s_xraw["o"][0], 16, c["owhi"])

            def c_step(it, u):
                n, k = it * 4 + u, u % 2
                h, hp = it * 2 + u // 2, (u // 2) % 2
                static = isinstance(n, int)
                more1, more2 = (not static or n + 1 < UNITS), (not static or n + 2 < UNITS)
                act.wait_ge(c["tr"], n + 1)
                copy(xpT[:, :, 0, :], XT_bank.rearrange("p (t n) -> p t n", t=4)).then_inc(c["pThi"], 1)
                if static and n == 0:
                    residual(1)
                vs = (u % 4 == 0 and not (static and n == 0)) or (u % 4 == 3 and more1)
                if vs:
                    vhalf = 1 if u % 4 == 0 else 0
                    cnt = (it + u // 4) * 4 + (2 if vhalf else 4)
                    v_evac(vhalf, 0, cnt + 1)
                if more1:
                    c_exps(n + 1, 1 - k)
                if more2:
                    act.wait_ge(c["q"], n + 3)
                    copy(xq_hi[:, k], XQ_bank).then_inc(c["qhi"], 1)
                if vs:
                    v_evac(vhalf, 1, cnt + 2)
                act.wait_ge(c["pv"], n + 1)
                copy(xo[:, 0], XO_bank[:, :, 0:P]).then_inc(c["ohi"], 1)
                act.wait_ge(c["osum"], n + 1)
                copy(xoT_hi[:, k].rearrange("p (t n) -> p t n", t=4), xo[:, 1]).then_inc(c["oThi"], 1)
                if more2:
                    k_evac(n + 2, k, n + 3)
                if k == 0 and (not static or h + 2 < NH):
                    loads = (it + u // 4 + 2) * 16
                    raw_split(xwq_hi[:, hp], xwq_raw[:, hp], s_xraw["q"][hp], loads, c["qwhi"])
                    raw_split(xwk_hi[:, hp], xwk_raw[:, hp], s_xraw["k"][hp], loads, c["kwhi"])
                if k == 1 and (not static or h + 1 < NH):
                    raw_split(xwo_hi[:, 1 - hp], xwo_raw[:, 1 - hp], s_xraw["o"][1 - hp],
                              (it + (u // 2 + 1) // 2 + 1) * 16, c["owhi"])
                if u % 4 == 1 and (not static or it + u // 4 + 1 < NH // 2):
                    raw_split(xwv_hi[:, :, :], xwv_raw[:, :, :], s_xvraw, (it + u // 4 + 2) * 16, c["vwhi"])
                if static and n == UNITS - 2:
                    for h_ in range(2):
                        raw_split(w1_hi[:, h_], w1_raw[:, h_], s_w1raw[h_], 16, f["w1hi"])
                    raw_split(w2_hi[:, 0], w2_raw[:, 0], s_w2raw[0], 16, f["w2hi"])

            c_step(0, 0)
            with act.Fori(0, 14) as it:
                for u in range(1, 5):
                    c_step(it, u)
            for u in range(1, 8):
                c_step(14, u)

            ln_sqrt(3, 1)
            ln_hi(3, 0)
            ln_sqrt(3, 2)

            def gelu(n, k, hp, loads):
                act.wait_ge(s_b1[hp], loads)
                act.wait_ge(f["h"], n + 1)
                s.activation(hid[:, k], H_bank[k], ACT.Gelu_apprx_tanh, bias=b1_sb[:, hp:hp + 1],
                             scale=1.0).then_inc(f["gelu"], 1)
                act.wait_ge(f["gelu"], n + 1)
                copy(hid_hi[:, k], hid[:, k]).then_inc(f["hhi"], 1)

            ln_hi(3, 1)
            gelu(0, 0, 0, 16)

            def f_step(it, u):
                n, k = it * 4 + u, u % 2
                h, hp = it * 2 + u // 2, (u // 2) % 2
                static = isinstance(n, int)
                if not static or n + 1 < FUNITS:
                    gelu(n + 1, 1 - k, ((u + 1) // 2) % 2, (it + (u + 1) // 4 + 1) * 16)
                if k == 0 and (not static or h + 2 < NF):
                    act.wait_ge(f["h"], n + 2)
                    raw_split(w1_hi[:, hp], w1_raw[:, hp], s_w1raw[hp], (it + u // 4 + 2) * 16, f["w1hi"])
                if k == 1 and (not static or h + 1 < NF):
                    raw_split(w2_hi[:, 1 - hp], w2_raw[:, 1 - hp], s_w2raw[1 - hp],
                              (it + (u // 2 + 1) // 2 + 1) * 16, f["w2hi"])

            f_step(0, 0)
            with act.Fori(0, 6) as it:
                for u in range(1, 5):
                    f_step(it, u)
            for u in range(1, 8):
                f_step(6, u)

        @block.vector
        def _(dve):
            v = nc.vector
            chain = [0]

            def link(ins):
                chain[0] += 1
                ins.then_inc(s_dve, 1)
                dve.wait_ge(s_dve, chain[0])

            def newton(p, cnt, sl, dst):
                dve.wait_ge(L[p, "sqrt"], cnt)
                link(v.reciprocal(nrm[:, 2, sl], nrm[:, 1, sl]))
                link(v.tensor_tensor(nrm[:, 3, sl], nrm[:, 2, sl], nrm[:, 2, sl], ALU.mult))
                link(v.tensor_tensor(nrm[:, 4, sl], nrm[:, 3, sl], nrm[:, 0, sl], ALU.mult))
                link(v.tensor_scalar(nrm[:, 3, sl], nrm[:, 4, sl], -0.5, 1.5, ALU.mult, ALU.add))
                link(v.tensor_tensor(nrm[:, dst, sl], nrm[:, 2, sl], nrm[:, 3, sl], ALU.mult))

            def ln_stats(half):
                for b in range(4 * half, 4 * half + 4):
                    last = v.bn_stats(stats[:, b, :], xacc[:, b, :])
                link(last)

            def layernorm(p, xn, half, meanwhile=None):
                sl = slice(4 * half, 4 * half + 4)
                cnt = (2 if p == 2 else 1) * half
                for b in range(4 * half, 4 * half + 4):
                    last = v.bn_aggr(meanvar[:, b, :], stats[:, b, :])
                link(last)
                v.tensor_scalar(nrm[:, 0, sl], meanvar[:, sl, 1], EPS, None, ALU.add).then_inc(L[p, "stat"], 1)
                if p == 2:
                    for b in range(4 * half, 4 * half + 4):
                        v.scalar_tensor_tensor(xn[:, b, :], xacc[:, b, :], meanvar[:, b, 0:1], lnw_sb[:, :],
                                               ALU.subtract, ALU.mult).then_inc(s_xl, 1)
                if meanwhile:
                    meanwhile()
                newton(p, cnt + 1, sl, 5)
                if p == 2:
                    link(v.tensor_tensor(nrm[:, 6, sl], nrm[:, 5, sl], nrm[:, 5, sl], ALU.mult))
                    link(v.tensor_tensor(nrm[:, 6, sl], nrm[:, 6, sl], meanvar[:, sl, 1], ALU.mult))
                    v.tensor_scalar(nrm[:, 0, sl], nrm[:, 6, sl], EPS, None, ALU.add).then_inc(L[p, "stat"], 1)
                    newton(p, cnt + 2, sl, 7)
                    v.tensor_scalar(nrm[:, 8, sl], nrm[:, 5, sl], 1.0, None, ALU.add)
                    v.scalar_tensor_tensor(nrm[:, 9, sl], meanvar[:, sl, 0], -1.0, nrm[:, 5, sl],
                                           ALU.mult, ALU.mult)
                    v.tensor_tensor(nrm[:, 6, sl], nrm[:, 5, sl], nrm[:, 7, sl], ALU.mult).then_inc(s_factor, 1)
                else:
                    for b in range(4 * half, 4 * half + 4):
                        v.tensor_scalar(xn[:, b, :], xacc[:, b, :], meanvar[:, b, 0:1],
                                        nrm[:, 5, b:b + 1], ALU.subtract, ALU.mult).then_inc(L[p, "xn"], 1)

            def ln_lo(p, half):
                for b in range(4 * half, 4 * half + 4):
                    dve.wait_ge(L[p, "hi"], b + 1)
                    v.tensor_tensor(xT_lo[:, :, b * P:(b + 1) * P],
                                    bank[:, ln_bank(p, b), :].rearrange("p (c n) -> p c n", c=C),
                                    xT_hi[:, :, b * P:(b + 1) * P], ALU.subtract).then_inc(L[p, "lo"], 1)

            dve.wait_ge(s_rope_in, 32)
            v.tensor_copy(rope[:, 0, 64:P], rope[:, 0, 0:64])
            link(v.tensor_copy(rope[:, 1, 64:P], rope[:, 1, 0:64]))
            link(v.tensor_scalar(rope[:, 1, 0:64], rope[:, 1, 0:64], -1.0, None, ALU.mult))
            v.tensor_scalar(ropeq[:, :, :], rope[:, :, :], SCALE, None, ALU.mult).then_inc(s_rope, 1)
            for half in range(2):
                for b in range(4 * half, 4 * half + 4):
                    dve.wait_ge(s_x[b], 16)
                ln_stats(half)
                layernorm(1, xn1, half)
                if half == 0:
                    ln_lo(1, 0)

            def kv_split(m):
                dve.wait_ge(s_kvhi, m + 1)
                v.tensor_tensor(kv_stage[m % 2][1][:, :, :], kv_raw[:, m % 2], kv_stage[m % 2][0][:, :, :],
                                ALU.subtract).then_inc(s_kvlo, 1)

            def k_rope(m):
                dve.wait_ge(s_kvmm, m + 1)
                src = bank[:, 4 + m % 2, :].rearrange("p (g e n) -> p g e n", g=4, e=2)
                t_cos = knew[:, 0, :].rearrange("p (g e n) -> p g e n", g=4, e=2)
                t_sin = knew[:, 1, :].rearrange("p (g e n) -> p g e n", g=4, e=2)
                if m:
                    dve.wait_ge(s_ktr, m)
                for e in range(2):
                    cos = rope[:, 0, e * 64:(e + 1) * 64].unsqueeze(1).to_broadcast([P, 4, 64])
                    sin = rope[:, 1, e * 64:(e + 1) * 64].unsqueeze(1).to_broadcast([P, 4, 64])
                    v.tensor_tensor(t_cos[:, :, e, :], src[:, :, e, :], cos, ALU.mult)
                    last = v.tensor_tensor(t_sin[:, :, e, :], src[:, :, 1 - e, :], sin, ALU.mult)
                link(last)
                v.tensor_tensor(knew[:, 2, :], knew[:, 0, :], knew[:, 1, :], ALU.add).then_inc(s_knew, 1)

            def q_lo_evac(k, cnt):
                dve.wait_ge(a["qhi"], cnt)
                v.tensor_tensor(q_lo[:, k], M_bank, q_hi[:, k], ALU.subtract).then_inc(a["qlo"], 1)

            kv_split(0)
            q_lo_evac(0, 1)
            ln_lo(1, 1)
            kv_split(1)
            q_lo_evac(1, 2)
            for m in range(2, 4):
                k_rope(m - 2)
                kv_split(m)

            def kv_group(grp, slot, cnt):
                dve.wait_ge(a["Khi"], cnt)
                v.tensor_tensor(K_lo[:, slot].rearrange("p (b t) -> p b t", t=BLOCK), K_all[:, :, grp, :],
                                K_hi[:, slot].rearrange("p (b t) -> p b t", t=BLOCK),
                                ALU.subtract).then_inc(a["Klo"], 1)
                dve.wait_ge(a["Vhi"], cnt)
                v.tensor_tensor(V_lo[:, slot], V_all[:, :, bass.ds(grp * P, P)] if not isinstance(grp, int)
                                else V_all[:, :, grp * P:(grp + 1) * P],
                                V_hi[:, slot], ALU.subtract).then_inc(a["Vlo"], 1)

            def maxes(n, slot, i):
                dve.wait_ge(a["S"], 4 * n + i + 1)
                v.tensor_reduce(negmax[:, slot, i:i + 1], S_bank[i % 2], mybir.AxisListType.XY, ALU.max,
                                negate=True).then_inc(a["max"], 1)

            def out_lo(n):
                dve.wait_ge(a["oThi"], n)
                v.tensor_tensor(oT_lo[:, :], O_bank, oT_hi[:, :], ALU.subtract).then_inc(a["oTlo"], 1)

            def accumulate(sems, m, k, half, i, M, cnt):
                dve.wait_ge(sems["wo"], 4 * m + i + 1)
                v.scalar_tensor_tensor(xacc[:, 4 * half + i, :], M, rinv[:, k, i:i + 1],
                                       xacc[:, 4 * half + i, :], ALU.mult, ALU.add).then_inc(sems["y"], 1)

            kv_group(0, 0, 1)
            for i in range(4):
                maxes(0, 0, i)

            def a_step(it, u):
                n, k = it * 8 + u, u % 2
                static = isinstance(n, int)
                more1, more2 = (not static or n + 1 < UNITS), (not static or n + 2 < UNITS)
                first = static and n == 0
                for j in range(KT):
                    if j < 4 and more1:
                        maxes(n + 1, 1 - k, j)
                    if j == 0:
                        if not first:
                            out_lo(n)
                        dve.wait_ge(a["exp"], 4 * n + 4)
                        v.reciprocal(rinv[:, k, :], rowsum[:, k, :]).then_inc(a["rinv"], 1)
                        if more2:
                            dve.wait_ge(a["qhi"], n + 3)
                            v.tensor_tensor(q_lo[:, k], M_bank, q_hi[:, k], ALU.subtract).then_inc(a["qlo"], 1)
                    elif not first:
                        if j == 1:
                            dve.wait_ge(a["rinv"], n)
                        accumulate(a, n - 1, 1 - k, 1 - k, j - 1, M_bank, None)
                    dve.wait_ge(a["pThi"], KT * n + j + 1)
                    v.tensor_tensor(pT_lo[:, j, :], T_bank[j % 2 if k == 0 else (j + 1) % 2], pT_hi[:, j, :],
                                    ALU.subtract).then_inc(a["pTlo"], 1)
                if u % 4 == 1 and (not static or n // 4 + 1 < UNITS // 4):
                    kv_group(it + (u // 4 + 1) // 2, (u // 4 + 1) % 2, it * 2 + u // 4 + 2)

            a_step(0, 0)
            with dve.Fori(0, 7) as it:
                for u in range(1, 9):
                    a_step(it, u)
            for u in range(1, 8):
                a_step(7, u)
            out_lo(UNITS)
            dve.wait_ge(a["rinv"], UNITS)
            dve.wait_ge(a["y"], LAST1 - 4)
            ln_stats(0)
            for i in range(4):
                accumulate(a, UNITS - 1, 1, 1, i, bank[:, i, :], None)

            def v_evac(half, j, cnt):
                dve.wait_ge(c["vhi"], cnt)
                v.tensor_tensor(xV_lo[:, half, 2 * j:2 * j + 2, :], XV_bank.rearrange("p (t n) -> p t n", t=2),
                                xV_hi[:, half, 2 * j:2 * j + 2, :], ALU.subtract).then_inc(c["vlo"], 1)

            def xq_lo_evac(k, cnt):
                dve.wait_ge(c["qhi"], cnt)
                v.tensor_tensor(xq_lo[:, k], XQ_bank, xq_hi[:, k], ALU.subtract).then_inc(c["qlo"], 1)

            def xk_lo_evac(k, cnt):
                dve.wait_ge(c["khi"], cnt)
                v.tensor_tensor(xk[:, k, :, 1, :], XK_bank.rearrange("p (t n) -> p t n", t=4), xk[:, k, :, 0, :],
                                ALU.subtract).then_inc(c["klo"], 1)

            dve.wait_ge(s_lnw, 16)
            layernorm(2, xn2, 0, meanwhile=lambda: v_evac(0, 0, 1))
            dve.wait_ge(a["y"], LAST1)
            ln_stats(1)
            v_evac(0, 1, 2)
            xk_lo_evac(0, 1)
            ln_lo(2, 0)
            v_evac(1, 0, 3)
            layernorm(2, xn2, 1, meanwhile=lambda: xk_lo_evac(1, 2))
            xq_lo_evac(0, 1)
            ln_lo(2, 1)

            def c_score(n, slot, half):
                dve.wait_ge(c["S"], n + 1)
                dve.wait_ge(c["comb"], n + 1)
                v.tensor_tensor(xscore[:, slot], XS_bank[:, :, 0:P], comb[:, half], ALU.add).then_inc(c_s1, 1)
                dve.wait_ge(c_s1, n + 1)
                v.tensor_tensor(xscore[:, slot], XS_bank[:, :, P:2 * P], xscore[:, slot], ALU.add)\
                 .then_inc(c["score"], 1)
                dve.wait_ge(c["score"], n + 1)
                v.tensor_reduce(negmax[:, slot, :], xscore[:, slot], AX_X, ALU.max, negate=True)\
                 .then_inc(c["max"], 1)

            c_score(0, 0, 0)
            v_evac(1, 1, 4)
            xq_lo_evac(1, 2)
            dve.wait_ge(s_mask, 16)
            link(v.tensor_reduce(anykey[:, :], mask_sb[:, :, :], AX_X, ALU.max))

            def c_step(it, u):
                n, k = it * 4 + u, u % 2
                static = isinstance(n, int)
                more1, more2 = (not static or n + 1 < UNITS), (not static or n + 2 < UNITS)
                first = static and n == 0

                def acc(i):
                    if not first:
                        accumulate(c, n - 1, 1 - k, 1 - k, i, (XW_last if static and not more2 else XW_bank)[i], None)

                dve.wait_ge(c["pThi"], n + 1)
                v.tensor_tensor(xpT[:, :, 1, :], XT_bank.rearrange("p (t n) -> p t n", t=4), xpT[:, :, 0, :],
                                ALU.subtract).then_inc(c["pTlo"], 1)
                if more1:
                    c_score(n + 1, 1 - k, 1 - k)
                vs = (u % 4 == 0 and not first) or (u % 4 == 3 and more1)
                if vs:
                    vhalf = 1 if u % 4 == 0 else 0
                    cnt = (it + u // 4) * 4 + (2 if vhalf else 4)
                    v_evac(vhalf, 0, cnt + 1)
                if not first:
                    dve.wait_ge(c["rinv"], n)
                acc(0)
                if not static or n > 1:
                    dve.wait_ge(c["y"], 4 * n - 4)
                dve.wait_ge(c["exp"], 4 * n + 4)
                v.reciprocal(rinv[:, k, :], rowsum[:, k, :]).then_inc(c_r1, 1)
                if more2:
                    dve.wait_ge(c["qhi"], n + 3)
                    v.tensor_tensor(xq_lo[:, k], XQ_bank, xq_hi[:, k], ALU.subtract).then_inc(c["qlo"], 1)
                dve.wait_ge(c_r1, n + 1)
                v.tensor_tensor(rinv[:, k, :], rinv[:, k, :], anykey[:, 4 * k:4 * k + 4], ALU.mult)\
                 .then_inc(c["rinv"], 1)
                if vs:
                    v_evac(vhalf, 1, cnt + 2)
                acc(1)
                dve.wait_ge(c["ohi"], n + 1)
                v.tensor_tensor(xo[:, 1], XO_bank[:, :, P:2 * P], xo[:, 0], ALU.add)\
                 .then_inc(c["osum"], 1)
                if not more1:
                    acc(2)
                dve.wait_ge(c["oThi"], n + 1)
                v.tensor_tensor(xoT_lo[:, k].rearrange("p (t n) -> p t n", t=4), xo[:, 1],
                                xoT_hi[:, k].rearrange("p (t n) -> p t n", t=4),
                                ALU.subtract).then_inc(c["oTlo"], 1)
                if more2:
                    xk_lo_evac(k, n + 3)
                if more1:
                    acc(2)
                acc(3)

            c_step(0, 0)
            dve.wait_ge(c["res"], B)
            with dve.Fori(0, 14) as it:
                for u in range(1, 5):
                    c_step(it, u)
            for u in range(1, 8):
                c_step(14, u)
            dve.wait_ge(c["rinv"], UNITS)
            dve.wait_ge(c["y"], LAST1 - 4)
            ln_stats(0)

            def last_outputs():
                for i in range(4):
                    accumulate(c, UNITS - 1, 1, 1, i, bank[:, 4 + i, :], None)

            layernorm(3, xn3, 0, meanwhile=last_outputs)
            dve.wait_ge(c["y"], LAST1)
            ln_stats(1)
            layernorm(3, xn3, 1, meanwhile=lambda: ln_lo(3, 0))

            def h_lo(n, k):
                dve.wait_ge(f["hhi"], n + 1)
                v.tensor_tensor(hid_lo[:, k], hid[:, k], hid_hi[:, k], ALU.subtract).then_inc(f["hlo"], 1)

            ln_lo(3, 1)
            h_lo(0, 0)
            dve.wait_ge(s_y0, 1)

            def f_step(it, u):
                n, k = it * 4 + u, u % 2
                static = isinstance(n, int)
                for i in range(4):
                    if i == 2 and (not static or n + 1 < FUNITS):
                        h_lo(n + 1, 1 - k)
                    dve.wait_ge(f["y"], 4 * n + i + 1)
                    t = 4 * k + i
                    v.tensor_tensor(yacc[:, t, :], Y_bank[i], yacc[:, t, :], ALU.add).then_inc(f["acc"], 1)

            f_step(0, 0)
            with dve.Fori(0, 6) as it:
                for u in range(1, 5):
                    f_step(it, u)
            for u in range(1, 8):
                f_step(6, u)
            dve.wait_ge(s_xb, B)
            for b in range(B):
                if b % 4 == 0:
                    dve.wait_ge(f["acc"], 4 * FUNITS - (4 if b < 4 else 0))
                v.tensor_scalar(finite[:, b, :], yacc[:, b, :], 0.0, 0.0, ALU.mult, ALU.is_equal)\
                 .then_inc(f["finite"], 1)
            for b in range(B):
                dve.wait_ge(f["finite"], b + 1)
                dve.wait_ge(f["sum"], b + 1)
                v.copy_predicated(xacc[:, b, :], finite[:, b, :], ysum[:, b, :]).then_inc(f["fin"], 1)

        @block.tensor
        def _(pe):
            t = nc.tensor

            def mm3(dst, w, m, start, stop):
                t.matmul(dst, w[0], m[0], start=start, stop=False)
                t.matmul(dst, w[0], m[1], start=False, stop=False)
                return t.matmul(dst, w[1], m[0], start=False, stop=stop)

            def project(dst, w, act_, cols):
                for ch in range(C):
                    last = mm3(dst, [z[:, ch, :] for z in w], [z[:, ch, cols] for z in act_],
                               ch == 0, ch == C - 1)
                return last

            xT = (xT_hi, xT_lo)

            def ln_transpose(p, xn, half):
                for b in range(4 * half, 4 * half + 4):
                    pe.wait_ge(L[p, "xn"], b + 1)
                    if p < 3 and b >= 4:
                        pe.wait_ge(L[p, "lo"], b - 3)
                    for ch in range(C):
                        last = t.transpose(bank[:, ln_bank(p, b), ch * P:(ch + 1) * P], xn[:, b, ch * P:(ch + 1) * P],
                                           ident[:, :])
                    last.then_inc(L[p, "tr"], 1)

            pe.wait_ge(s_ident, 1)
            def k_transpose(m):
                pe.wait_ge(s_knew, m + 1)
                if m:
                    pe.wait_ge(s_kvev, m)
                for g_ in range(4):
                    last = t.transpose(bank[:, 6, g_ * P:(g_ + 1) * P], knew[:, 2, g_ * P:(g_ + 1) * P], ident[:, :])
                last.then_inc(s_ktr, 1)

            def queries(m, h, hp, half):
                pe.wait_ge(a["wqlo"], h + 1)
                project(M_bank, [z[:, hp] for z in (wq_hi, wq_lo)], xT,
                        slice(half * HALF, (half + 1) * HALF)).then_inc(a["q"], 1)

            for half in range(2):
                ln_transpose(1, xn1, half)
                pe.wait_ge(L[1, "lo"], 4 * half + 4)
                if half:
                    pe.wait_ge(a["qlo"], 1)
                queries(half, 0, 0, half)
            for m in range(4):
                pe.wait_ge(s_kvlo, m + 1)
                if m >= 2:
                    pe.wait_ge(s_knew, m - 1)
                for ch in range(C):
                    last = mm3(bank[:, 4 + m % 2, :], [z[:, ch, 0:P] for z in xT],
                               [z[:, ch, :] for z in kv_stage[m % 2]], ch == 0, ch == C - 1)
                last.then_inc(s_kvmm, 1)
                if m >= 1 and m <= 2:
                    k_transpose(m - 1)

            def scores(n, k, ks, i):
                cols = slice(i * P, (i + 1) * P)
                K = (K_hi, K_lo)
                for j, (w, m) in enumerate(((q_hi, 0), (q_hi, 1), (q_lo, 0))):
                    for hf in range(2):
                        last = t.matmul(S_bank[i % 2][:, hf, :], w[:, k, cols], K[m][:, ks, hf * TH:(hf + 1) * TH],
                                        start=(j == 0), stop=(j == 2))
                last.then_inc(a["S"], 1)

            pe.wait_ge(a["Klo"], 1)
            for i in range(4):
                if i >= 2:
                    pe.wait_ge(a["exp"], i - 1)
                scores(0, 0, 0, i)

            def a_out(m, hp, i, M):
                last = mm3(M, [z[:, i * P:(i + 1) * P] for z in (oT_hi, oT_lo)],
                           [z[:, hp, :] for z in (wo_hi, wo_lo)], True, True)
                last.then_inc(a["wo"], 1)

            def a_step(it, u):
                n, k = it * 8 + u, u % 2
                h = it * 4 + u // 2
                static = isinstance(n, int)
                more1, more2 = (not static or n + 1 < UNITS), (not static or n + 2 < UNITS)
                first = static and n == 0
                ks = (u // 4) % 2
                for j in range(KT):
                    if j < 4 and more1:
                        if j == 0:
                            pe.wait_ge(a["qlo"], n + 2)
                            if u % 4 == 3:
                                pe.wait_ge(a["Klo"], it * 2 + u // 4 + 2)
                        pe.wait_ge(a["exp"], 4 * n + 4 + j - 1)
                        scores(n + 1, 1 - k, ((u + 1) // 4) % 2, j)
                    if j == 0:
                        if not first:
                            pv(n - 1, 1 - k, ((u - 1) // 4) % 2, KT - 1, it, u - 1)
                        if more2:
                            if first:
                                pe.wait_ge(a["qlo"], 2)
                            elif not static or n > 1:
                                pe.wait_ge(a["y"], 4 * n - 4)
                            queries(n + 2, h + 1, ((u + 2) // 2) % 2, k)
                    if j == 0:
                        pe.wait_ge(a["exp"], 4 * n + 4)
                    if not (first and j < 2):
                        pe.wait_ge(a["pTlo"], KT * n + j - 1)
                    for i in range(4):
                        last = t.transpose(T_bank[j % 2 if k == 0 else (j + 1) % 2][:, i * P:(i + 1) * P],
                                           prob[:, k, i, j * P:(j + 1) * P], ident[:, :])
                    last.then_inc(a["tr"], 1)
                    if j and not first:
                        if j == 1:
                            pe.wait_ge(a["oTlo"], n)
                            pe.wait_ge(a["qlo"], min(n + 3, UNITS) if static else n + 3)
                            if k == 1:
                                pe.wait_ge(a["wolo"], h + 1)
                        else:
                            pe.wait_ge(a["y"], 4 * n - 4 + j - 1)
                        a_out(n - 1, ((u - 1) // 2) % 2, j - 1, M_bank)
                    if j:
                        pv(n, k, ks, j - 1, it, u)

            def pv(n, k, ks, j, it, u):
                if j == 0:
                    if not isinstance(n, int) or n:
                        pe.wait_ge(a["oTlo"], n)
                    if u % 4 == 0:
                        pe.wait_ge(a["Vlo"], it * 2 + u // 4 + 1)
                pe.wait_ge(a["pTlo"], KT * n + j + 1)
                last = mm3(O_bank, [z[:, ks, j, :] for z in (V_hi, V_lo)], [z[:, j, :] for z in (pT_hi, pT_lo)],
                           j == 0, j == KT - 1)
                if j == KT - 1:
                    last.then_inc(a["pv"], 1)

            for u in range(9):
                a_step(0, u)
            with pe.Fori(1, 7) as it:
                for u in range(1, 9):
                    a_step(it, u)
            for u in range(1, 8):
                a_step(7, u)
            pv(UNITS - 1, 1, 1, KT - 1, 7, 7)
            pe.wait_ge(a["oTlo"], UNITS)
            for i in range(4):
                a_out(UNITS - 1, 1, i, bank[:, i, :])

            cT = (cT_hi, cT_lo)

            def values(half, j, cnt):
                if not isinstance(cnt, int) or cnt > 0:
                    pe.wait_ge(c["vlo"], cnt)
                for tt in range(2):
                    tok = (4 * half + 2 * j + tt) * P
                    for ch in range(C):
                        last = mm3(XV_bank[:, tt * 2 * P:(tt + 1) * 2 * P], [z[:, ch, tok:tok + P] for z in cT],
                                   [z[:, ch, :] for z in (xwv_hi, xwv_lo)], ch == 0, ch == C - 1)
                last.then_inc(c["v"], 1)

            def c_queries(h, hp, half):
                pe.wait_ge(c["qwlo"], h + 1)
                project(XQ_bank, [z[:, hp] for z in (xwq_hi, xwq_lo)], xT,
                        slice(half * HALF, (half + 1) * HALF)).then_inc(c["q"], 1)

            def c_keys(h, hp, half):
                pe.wait_ge(c["kwlo"], h + 1)
                project(XK_bank, [z[:, hp] for z in (xwk_hi, xwk_lo)], cT,
                        slice(half * HALF, (half + 1) * HALF)).then_inc(c["k"], 1)

            def c_scores(n, k):
                pe.wait_ge(c["qlo"], n + 1)
                pe.wait_ge(c["klo"], n + 1)
                for i in range(4):
                    cols = slice(i * P, (i + 1) * P)
                    t.matmul(XS_bank[:, i, :], xq_hi[:, k, cols], xk[:, k, i], start=True, stop=False)
                    last = t.matmul(XS_bank[:, i, :], xq_lo[:, k, cols], xk[:, k, i], start=False, stop=True)
                last.then_inc(c["S"], 1)

            pe.wait_ge(s_clo, C)
            pe.wait_ge(c["vwlo"], 1)
            values(0, 0, 0)
            values(0, 1, 1)
            c_keys(0, 0, 0)
            ln_transpose(2, xn2, 0)
            values(1, 0, 2)
            pe.wait_ge(c["klo"], 1)
            c_keys(0, 0, 1)
            pe.wait_ge(L[2, "lo"], 4)
            c_queries(0, 0, 0)
            values(1, 1, 3)
            ln_transpose(2, xn2, 1)
            pe.wait_ge(L[2, "lo"], B)
            c_scores(0, 0)
            pe.wait_ge(c["qlo"], 1)
            c_queries(0, 0, 1)

            def c_out(k, hp, i, M):
                last = mm3(M, [z[:, k, i * P:(i + 1) * P] for z in (xoT_hi, xoT_lo)],
                           [z[:, hp, :] for z in (xwo_hi, xwo_lo)], True, True)
                last.then_inc(c["wo"], 1)

            def c_step(it, u):
                n, k = it * 4 + u, u % 2
                h, hp = it * 2 + u // 2, (u // 2) % 2
                static = isinstance(n, int)
                more1, more2 = (not static or n + 1 < UNITS), (not static or n + 2 < UNITS)
                first = static and n == 0

                def o(i):
                    if not first:
                        if i == 0:
                            pe.wait_ge(c["oTlo"], n)
                            if k == 1:
                                pe.wait_ge(c["owlo"], h + 1)
                        if static and not more2 and i in (1, 2):
                            pe.wait_ge(*((c["klo"], UNITS) if i == 1 else (c["vlo"], 2 * UNITS // 2)))
                        elif i == 3:
                            pe.wait_ge(c["qlo"], min(n + 3, UNITS) if static else n + 3)
                            if static and not more2:
                                pe.wait_ge(c["y"], 4 * n - 4)
                        elif i or not static or n > 1:
                            pe.wait_ge(c["y"], 4 * n - 4 + i if i else 4 * n - 5)
                        c_out(1 - k, ((u - 1) // 2) % 2, i,
                              (XW_last if static and not more2 else XW_bank)[i])

                pe.wait_ge(c["exp"], 4 * n + 4)
                if not first:
                    pe.wait_ge(c["osum"], n)
                for i in range(4):
                    last = t.transpose(XT_bank[:, i * P:(i + 1) * P], xprob[:, k, i, :], ident[:, :])
                last.then_inc(c["tr"], 1)
                if more1:
                    pe.wait_ge(c["score"], n + 1)
                    c_scores(n + 1, 1 - k)
                vs = (u % 4 == 0 and not first) or (u % 4 == 3 and more1)
                if vs:
                    vhalf = 1 if u % 4 == 0 else 0
                    cnt = (it + u // 4) * 4 + (2 if vhalf else 4)
                    if not vhalf:
                        pe.wait_ge(c["vwlo"], it + u // 4 + 2)
                    values(vhalf, 0, cnt)
                o(0)
                if more2:
                    pe.wait_ge(c["qlo"], n + 2)
                    if not static or n > 1:
                        pe.wait_ge(c["y"], 4 * n - 4)
                    c_queries(h + 1, 1 - hp, k)
                if vs:
                    values(vhalf, 1, cnt + 1)
                o(1)
                pe.wait_ge(c["pTlo"], n + 1)
                if u % 4 < 2:
                    pe.wait_ge(c["vlo"], (it + u // 4) * 4 + (2 if u % 4 == 0 else 4))
                for i in range(4):
                    t.matmul(XO_bank[:, i, :], xV_hi[:, k, i, hp * P:(hp + 1) * P], xpT[:, i], start=True, stop=False)
                    last = t.matmul(XO_bank[:, i, :], xV_lo[:, k, i, hp * P:(hp + 1) * P], xpT[:, i],
                                    start=False, stop=True)
                last.then_inc(c["pv"], 1)
                if more2:
                    pe.wait_ge(c["klo"], n + 2)
                    c_keys(h + 1, 1 - hp, k)
                o(2)
                o(3)

            for u in range(5):
                c_step(0, u)
            with pe.Fori(1, 14) as it:
                for u in range(1, 5):
                    c_step(it, u)
            for u in range(1, 8):
                c_step(14, u)
            pe.wait_ge(c["oTlo"], UNITS)
            pe.wait_ge(c["y"], LAST1 - 4)
            for i in range(4):
                c_out(1, 1, i, bank[:, 4 + i, :])

            ln_transpose(3, xn3, 0)
            pe.wait_ge(L[3, "lo"], 4)

            def hidden(n, h, hp, k):
                pe.wait_ge(f["w1lo"], h + 1)
                project(H_bank[k], [z[:, hp] for z in (w1_hi, w1_lo)], xT,
                        slice(k * HALF, (k + 1) * HALF)).then_inc(f["h"], 1)

            hidden(0, 0, 0, 0)
            ln_transpose(3, xn3, 1)
            pe.wait_ge(L[3, "lo"], B)

            def f_step(it, u):
                n, k = it * 4 + u, u % 2
                h, hp = it * 2 + u // 2, (u // 2) % 2
                static = isinstance(n, int)
                if not static or n + 1 < FUNITS:
                    if not static or n:
                        pe.wait_ge(f["hhi"], n)
                    hidden(n + 1, h + k, hp if k == 0 else 1 - hp, 1 - k)
                pe.wait_ge(f["hlo"], n + 1)
                if k == 0:
                    pe.wait_ge(f["w2lo"], h + 1)
                for i in range(4):
                    if not static or n:
                        pe.wait_ge(f["acc"], 4 * n - 4 + i + 1)
                    mm3(Y_bank[i], [z[:, k, i * P:(i + 1) * P] for z in (hid_hi, hid_lo)],
                        [z[:, hp, :] for z in (w2_hi, w2_lo)], True, True).then_inc(f["y"], 1)

            f_step(0, 0)
            with pe.Fori(0, 6) as it:
                for u in range(1, 5):
                    f_step(it, u)
            for u in range(1, 8):
                f_step(6, u)


def layouts(i):
    def heads(w, n):
        return w.reshape(n, P, C, P).transpose(0, 3, 2, 1)

    def rotated(w, n):
        return w.reshape(n, P // 2, 2, C, P).transpose(0, 4, 3, 2, 1)

    def four_heads(w):
        return w.reshape(2, D, C, P).transpose(0, 3, 2, 1)

    wk = i["L0_attn_wk"].reshape(2, 4, P // 2, 2, C, P).transpose(0, 5, 4, 1, 3, 2)
    return {
        "x": i["x"],
        "ctxT": i["ctx_4096"].reshape(TOK, C, P).transpose(2, 1, 0),
        "mask": i["mask_BxSxS2_bk0"].transpose(1, 0, 2),
        "fcos": i["L0_attn_freqs_cos"].reshape(P // 2),
        "fsin": i["L0_attn_freqs_sin"].reshape(P // 2),
        "wq": rotated(i["L0_attn_wq"], NH).reshape(NH, P, C, P),
        "wk": wk.reshape(2, P, C, D),
        "wv": four_heads(i["L0_attn_wv"]),
        "wo": i["L0_attn_wo"].transpose(1, 0).reshape(NH, P, D),
        "kc": i["L0_attn_k_cache"].reshape(NBLK, BLOCK, NKV, P // 2, 2).transpose(0, 4, 3, 2, 1)
                                  .reshape(NBLK, P, NKV, BLOCK),
        "vc": i["L0_attn_v_cache"].reshape(NBLK, BLOCK, NKV * P),
        "bidx": i["L0_attn_block_idx"].reshape(1, TOPK),
        "xbias": i["L0_xattn_position_bias"],
        "lnw": i["L0_xattn_ln_weight"],
        "xwq": heads(i["L0_xattn_w_q"], NH),
        "xwk": heads(i["L0_xattn_w_k"], NH),
        "xwv": i["L0_xattn_w_v"].reshape(NH // 2, 2 * P, C, P).transpose(0, 3, 2, 1),
        "xwo": i["L0_xattn_w_out"].transpose(1, 0).reshape(NH, P, D),
        "w1": i["L0_ffn_W1"].reshape(C, P, NF, P).transpose(2, 1, 0, 3),
        "b1": i["L0_ffn_b1"].reshape(NF, P, 1),
        "w2": i["L0_ffn_W2"].reshape(NF, P, D),
        "b2": i["L0_ffn_b2"],
    }


def kernel(**inputs):
    import numpy as np
    import concourse.bacc as bacc
    from concourse.bass_utils import run_bass_kernel_spmd

    nc = bacc.Bacc("TRN2", target_bir_lowering=False, num_devices=1)
    arrays, args = {}, []
    for name, a in layouts({k: np.asarray(v) for k, v in inputs.items()}).items():
        a = np.ascontiguousarray(a)
        arrays[f"in_{name}"] = a
        args.append(nc.dram_tensor(f"in_{name}", a.shape, mybir.dt.from_np(a.dtype), kind="ExternalInput").ap())
    out = nc.dram_tensor("out_x", (B, P, D), F32, kind="ExternalOutput").ap()
    decoder_layer(nc, *args, out)
    r = run_bass_kernel_spmd(nc, [arrays], core_ids=[0])
    return r.results[0]["out_x"]
```
